# Optimizing a Trainium2 kernel written in Bass

```python
import numpy as np
import jax
import jax.numpy as jnp

def _softmax(x, axis=-1):
    return jax.nn.softmax(x, axis=axis)

def _gelu(x):
    return jax.nn.gelu(x, approximate=True)

def _silu(x):
    return jax.nn.silu(x)

def _sigmoid(x):
    return jax.nn.sigmoid(x)

def _layernorm(x, axis=-1, eps=1e-05):
    m = jnp.mean(x, axis=axis, keepdims=True)
    v = jnp.var(x, axis=axis, keepdims=True)
    return (x - m) / jnp.sqrt(v + eps)

def _scatter_add(tgt, idx, src, axis=0):
    return tgt.at[idx].add(src)

def _segment_sum(src, seg, n):
    return jax.ops.segment_sum(src, seg, n)
kernel_name = 'mk_seq_postln_d1_jaxref_r8_c759ae'

def setup_inputs(seed: int=0):
    np.random.seed(seed)
    _w = jnp.asarray

    def _L0_attn_setup():
        import jax, jax.numpy as jnp
        import numpy as np
        D_MODEL = 128
        N_HEADS = 16
        WINDOW = 32
        SEQ = 512
        BATCH = 1
        NEG_INF = -1e+30
        key = jax.random.key(seed)
        ks = jax.random.split(key, 5)
        scale = 0.02
        inp = {'x': jax.random.normal(ks[0], (BATCH, SEQ, D_MODEL), jnp.float32)}
        for i, name in enumerate(['Wq', 'Wk', 'Wv', 'Wo']):
            inp[name] = jax.random.normal(ks[1 + i], (D_MODEL, D_MODEL), jnp.float32) * scale
        for name in ['bq', 'bk', 'bv', 'bo']:
            inp[name] = jnp.zeros((D_MODEL,), jnp.float32)
        return inp
    _L0_attn_in = _L0_attn_setup()

    def _L0_ffn_setup():
        import jax, jax.numpy as jnp
        import numpy as np
        B, S, D, E, F, TOP_K = (4, 256, 128, 8, 512, 2)
        key = jax.random.key(seed)
        k0, k1, k2, k3 = jax.random.split(key, 4)
        init = lambda k, shape, fan: (jax.random.normal(k, shape, jnp.float32) / np.sqrt(fan)).astype(jnp.float32)
        return {'x': jax.random.normal(k0, (B, S, D), jnp.float32), 'gate_w': init(k1, (D, E), D), 'w1': init(k2, (E, D, F), D), 'b1': jnp.zeros((E, F), jnp.float32), 'w2': init(k3, (E, F, D), F), 'b2': jnp.zeros((E, D), jnp.float32)}
    _L0_ffn_in = _L0_ffn_setup()
    _d = {'L0_attn_x': _L0_attn_in['x'], 'L0_attn_Wq': _L0_attn_in['Wq'], 'L0_attn_bq': _L0_attn_in['bq'], 'L0_attn_Wk': _L0_attn_in['Wk'], 'L0_attn_bk': _L0_attn_in['bk'], 'L0_attn_Wv': _L0_attn_in['Wv'], 'L0_attn_bv': _L0_attn_in['bv'], 'L0_attn_Wo': _L0_attn_in['Wo'], 'L0_attn_bo': _L0_attn_in['bo'], 'L0_ffn_gate_w': _L0_ffn_in['gate_w'], 'L0_ffn_w1': _L0_ffn_in['w1'], 'L0_ffn_b1': _L0_ffn_in['b1'], 'L0_ffn_w2': _L0_ffn_in['w2'], 'L0_ffn_b2': _L0_ffn_in['b2']}
    _x0 = _d['L0_attn_x']
    _d['L0_attn_x'] = jax.random.normal(jax.random.fold_in(jax.random.key(seed), 1), (32, 256, 128), dtype=_x0.dtype)
    del _x0
    return _d

def reference(L0_attn_x, L0_attn_Wq, L0_attn_bq, L0_attn_Wk, L0_attn_bk, L0_attn_Wv, L0_attn_bv, L0_attn_Wo, L0_attn_bo, L0_ffn_gate_w, L0_ffn_w1, L0_ffn_b1, L0_ffn_w2, L0_ffn_b2):

    def _L0_attn_ref(x, Wq, bq, Wk, bk, Wv, bv, Wo, bo):
        import jax, jax.numpy as jnp
        import numpy as np
        D_MODEL = 128
        N_HEADS = 16
        WINDOW = 32
        SEQ = 512
        BATCH = 1
        NEG_INF = -1e+30
        B, S, D = x.shape
        H = N_HEADS
        hd = D // H
        q = (x @ Wq + bq).reshape(B, S, H, hd).transpose(0, 2, 1, 3)
        k = (x @ Wk + bk).reshape(B, S, H, hd).transpose(0, 2, 1, 3)
        v = (x @ Wv + bv).reshape(B, S, H, hd).transpose(0, 2, 1, 3)
        scale = 1.0 / jnp.sqrt(jnp.asarray(hd, x.dtype))
        scores = jnp.einsum('bhqd,bhkd->bhqk', q, k) * scale
        i = jnp.arange(S)[:, None]
        j = jnp.arange(S)[None, :]
        allowed = (j <= i) & (i - j < WINDOW)
        scores = jnp.where(allowed, scores, NEG_INF)
        attn = jax.nn.softmax(scores, axis=-1)
        out = jnp.einsum('bhqk,bhkd->bhqd', attn, v)
        out = out.transpose(0, 2, 1, 3).reshape(B, S, D)
        return out @ Wo + bo

    def _L0_ffn_ref(x, gate_w, w1, b1, w2, b2):
        import jax, jax.numpy as jnp
        import numpy as np
        B, S, D, E, F, TOP_K = (4, 256, 128, 8, 512, 2)
        b, s, d = x.shape
        e = gate_w.shape[1]
        xf = x.reshape(-1, d)
        t = xf.shape[0]
        logits = xf @ gate_w
        top_w, top_idx = jax.lax.top_k(logits, TOP_K)
        top_w = jax.nn.softmax(top_w.astype(jnp.float32), axis=-1).astype(x.dtype)
        combine = jnp.zeros((t, e), x.dtype).at[jnp.arange(t)[:, None], top_idx].add(top_w)
        h = jax.nn.gelu(jnp.einsum('td,edf->tef', xf, w1) + b1, approximate=False)
        y = jnp.einsum('tef,efd->ted', h, w2) + b2
        out = jnp.einsum('ted,te->td', y, combine)
        return out.reshape(b, s, d)
    x = L0_attn_x
    x = _layernorm(x + _L0_attn_ref(x, L0_attn_Wq, L0_attn_bq, L0_attn_Wk, L0_attn_bk, L0_attn_Wv, L0_attn_bv, L0_attn_Wo, L0_attn_bo), axis=-1)
    x = _layernorm(x + _L0_ffn_ref(x, L0_ffn_gate_w, L0_ffn_w1, L0_ffn_b1, L0_ffn_w2, L0_ffn_b2), axis=-1)
    return x

_drawn_inputs = setup_inputs


def setup_inputs(seed=0):
    import zlib

    import numpy as np

    out = dict(_drawn_inputs(seed))
    spreads = {'L0_attn_bq': (0.0, 0.8),
     'L0_attn_bk': (0.0, 0.8),
     'L0_attn_bv': (0.0, 0.1),
     'L0_attn_bo': (0.0, 0.1),
     'L0_ffn_b1': (0.0, 0.1),
     'L0_ffn_b2': (0.0, 0.1)}
    factors = {'L0_attn_Wq': 7.801, 'L0_attn_Wk': 7.443}
    for name, (base, spread) in spreads.items():
        noise = np.random.default_rng([zlib.crc32(name.encode()), seed]).standard_normal(out[name].shape)
        drawn = base * np.exp(spread * noise) if base else spread * noise
        out[name] = jnp.asarray(drawn.astype(out[name].dtype))
    for name, factor in factors.items():
        out[name] = (out[name] * factor).astype(out[name].dtype)
    return out
```

```python
import numpy as np
import concourse.bass as bass
from concourse import mybir
from contextlib import ExitStack

U32, I32 = mybir.dt.uint32, mybir.dt.int32
FP32, FP16, BF16 = mybir.dt.float32, mybir.dt.float16, mybir.dt.bfloat16
ALU = mybir.AluOpType
ACT = mybir.ActivationFunctionType
AX = mybir.AxisListType

P = 128
B, S, D = 32, 256, 128
H, HD, WINDOW = 16, 8, 32
TILES = B * S // P
TPB = S // P
NJ = P // WINDOW
KEYS = 2 * WINDOW
HALF = H // 2
UP = 64.0
LIFT = 10 * float(np.log(2.0))
SCORE_SCALE = float(HD) ** -0.5 / (UP * UP)
NEG = -1e30
EPS = 1e-5
V_FLAT = [[64, 2], [32, 2], [1, 32]]
VW = HD * 4 + 1
V_DIAG = [[10 * VW, 2], [VW, 2], [1, VW - 1]]
BODY = 4
LAG_S, LAG_P, LAG_O, LAG_Y, LAG_R = 2, 3, 4, 5, 6
NE, F, TOPK = 8, 512, 2
TOKENS = B * S
NT = 256
NH = NT // P
FC = F // P
REGION = TOKENS + NT
SLOTS = TOKENS * TOPK // NT + NE
ROW = 132
C_ID, C_E1 = 128, 129
NOWHERE = float((1 << 20) // TOKENS)
WUP = 256.0
BUP = 128.0
CH = 4
CHUNKS = TILES // CH
T_TOK, T_BASE, T_E, T_PAD, T_SLOT = 0, TILES, TILES + NE, TILES + 2 * NE, TILES + 4 * NE
TAB_W = T_SLOT + 2 * SLOTS


def view(ap, dims, offset=0):
    return bass.AP(tensor=ap.tensor, offset=ap.offset + offset, ap=[ap.ap[0]] + dims)


def reach(eng, sem, n):
    if not isinstance(n, int) or n > 0:
        eng.wait_ge(sem, n)


def fixed(eng, v):
    return v if isinstance(v, int) else eng.snap(v)


def live(t):
    return not isinstance(t, int) or 0 <= t < TILES


def build(nc, x, wq, wk, wv, wo, bq, bk, bv, bo, gate_w, w1, b1, w2, b2, c_ident, c_seen, c_mask, c_heads, c_tri, c_tab, out):
    xt_dram = x.rearrange("b (t p) d -> p (b t) d", p=P)
    out_t = out.rearrange("b (t p) d -> p (b t) d", p=P)
    ctx = ExitStack()
    with ctx:
        def sb(name, shape, dt=FP32):
            return ctx.enter_context(nc.sbuf_tensor(name, shape, dt))

        def sem(name):
            return ctx.enter_context(nc.semaphore(name))

        stage = sb("stage", [P, 608])
        tab = sb("tab", [P, TAB_W])
        tri = sb("tri", [P, P], BF16)
        ones16 = sb("ones16", [P, P], BF16)
        ident = sb("ident", [P, P])
        ident16 = sb("ident16", [P, P], BF16)
        seen = sb("seen", [P, 2, P], BF16)
        mask = sb("mask", [P, HALF, KEYS], BF16)
        heads = sb("heads", [P, H, KEYS], BF16)
        Wq, Wk, Wv, Wo = (sb(n, [P, D]) for n in ("Wq", "Wk", "Wv", "Wo"))
        Wg = sb("Wg", [P, 8])
        qb = sb("qb", [P, 1])
        kb = sb("kb", [P, 1])
        vb_col = sb("vb_col", [P, 1])
        bo_row = sb("bo_row", [1, D])
        ones_row = sb("ones_row", [1, P])
        out_bias = sb("out_bias", [P, D])

        xin = sb("xin", [P, 2 * TPB, D])
        Y = sb("Y", [P, TILES, D])
        lg = sb("lg", [P, 2, NE])
        top = sb("top", [P, 2, 8])
        topi = sb("topi", [P, 2, 8], U32)
        hot = sb("hot", [P, 2, TOPK, NE])
        hot16 = sb("hot16", [P, 2, NE], BF16)
        seen16 = sb("seen16", [P, 2, NE], BF16)
        where = sb("where", [P, 2, NE])
        picked = sb("picked", [P, 2, TOPK, NE])
        pos = sb("pos", [P, BODY, TOPK], U32)
        vals = sb("vals", [P, TILES, TOPK])
        padrow = sb("padrow", [P, ROW])
        xT = sb("xT", [P, 2, S])
        q_hi = sb("q_hi", [P, 2, S], FP16)
        q_lo = sb("q_lo", [P, 2, S], FP16)
        k_nat = sb("k_nat", [P, 2, 2, S], FP16)
        KB_WORDS = 2 * 2 * H * (WINDOW + S) // 2
        area = sb("area", [P, KB_WORDS])
        KB = area[:, :].bitcast(FP16).rearrange("p (b q h c) -> p b q h c", b=2, q=2, h=H)
        taken = [0]

        def late(words, pattern, dt=FP32, **sizes):
            a = area[:, taken[0]:taken[0] + words]
            taken[0] += words
            return (a if dt == FP32 else a.bitcast(dt)).rearrange(pattern, **sizes)

        v_nat = sb("v_nat", [P, 2, TPB, 2, 2, 2, 2, VW], FP16)
        VB = sb("VB", [P, 2, TPB * NJ, 2, 2, 2, VW], FP16)
        E = sb("E", [P, 2, H * KEYS])
        PTh = sb("PTh", [P, 2, 2, NJ, P], FP16)
        PTl = sb("PTl", [P, 2, 2, NJ, P], FP16)
        nmax = sb("nmax", [P, 2, H])
        shift = sb("shift", [P, 2, P], BF16)
        shiftT = sb("shiftT", [P, 2, P], BF16)
        rec = sb("rec", [P, 2, 2, NJ * 2])
        O2 = sb("O2", [P, 2, 2, NJ, 16])
        attnT = sb("attnT", [P, 2, P])
        r1 = sb("r1", [P, 2, D])
        stats = sb("stats", [P, 2, 6])
        mv = sb("mv", [P, 2, 2])
        neg_half = sb("neg_half", [P, 1])
        turn = sb("turn", [P, 1])
        rstd = sb("rstd", [P, 2, 1])
        eps = sb("eps", [P, 1])
        var_eps = sb("var_eps", [P, 2, 1])
        yT = sb("yT", [P, 2, P])
        y_new = sb("y_new", [P, BODY, ROW])

        w_hi16, w_lo16 = (sb(n, [P, 2 * NE, F], FP16) for n in ("w_hi16", "w_lo16"))
        w1h, w1l = (w[:, 0:NE, :] for w in (w_hi16, w_lo16))
        w2h, w2l = (w[:, NE:2 * NE, :].rearrange("p e (c d) -> p e c d", c=FC) for w in (w_hi16, w_lo16))
        w_raw = sb("w_raw", [P, 2 * NE, F])
        wup = sb("wup", [P, 1])
        b1t = sb("b1t", [P, NE, FC])
        b2h = sb("b2h", [P, NE, D], FP16)
        b2raw = sb("b2raw", [64, NE, D])
        ones2 = sb("ones2", [P, P], FP16)
        count = sb("count", [P, NE])
        padpos = sb("padpos", [P, NH, NE], U32)
        ones_f = sb("ones_f", [P, 1])
        nt_i = sb("nt_i", [P, NE], I32)
        nt_s = sb("nt_s", [P, NE], I32)
        nt = sb("nt", [P, NE])
        ntc = sb("ntc", [P, NE])
        step_rows = sb("step_rows", [P, NE])
        past = sb("past", [P, NE, SLOTS])
        expert = sb("expert", [P, SLOTS])
        expert_i = sb("expert_i", [P, SLOTS], I32)
        start_f = sb("start_f", [P, 2, SLOTS])
        start_i = sb("start_i", [P, SLOTS], I32)
        wts = sb("wts", [P, TILES, TOPK])
        wtmp = sb("wtmp", [P, 4, TILES])
        xg = late(2 * NH * ROW, "p (b n c) -> p b n c", b=2, n=NH)
        xh, xl = (sb(n, [P, 2, NT], FP16) for n in ("xh", "xl"))
        G = late(2 * FC * NT, "p (b c t) -> p b c t", b=2, c=FC)
        Hh, Hl = (late(FC * NT, "p (b c t) -> p b c t", FP16, b=2, c=FC) for n in range(2))
        dst_f = sb("dst_f", [P, 2, NH])
        dst = sb("dst", [P, 2, NH], U32)
        zrow = sb("zrow", [P, 2, NH, D])
        zin = late(2 * TOPK * CH * D, "p (b k n d) -> p b k n d", b=2, k=TOPK, n=CH)
        zsum = late(2 * CH * D, "p (b n d) -> p b n d", b=2, n=CH)
        st2 = sb("st2", [P, 2, CH, 6])
        mv2 = sb("mv2", [P, 2, CH, 2])
        var2 = sb("var2", [P, 2, CH])
        rstd2 = sb("rstd2", [P, 2, CH])
        yout = late(2 * CH * D, "p (b n d) -> p b n d", b=2, n=CH)

        pS = ctx.enter_context(nc.psum_tensor("pS", [P, 2, 512], FP32))
        pT = ctx.enter_context(nc.psum_tensor("pT", [P, 2, 512], FP32))
        pO = ctx.enter_context(nc.psum_tensor("pO", [P, 2, 512], FP32))
        pC = ctx.enter_context(nc.psum_tensor("pC", [P, 512], FP32))
        pM = ctx.enter_context(nc.psum_tensor("pM", [P, 512], FP32))
        VROW = 2 * 2 * 2 * 2 * VW
        vwin = nc.dram_tensor("vwin", (2, WINDOW + S, VROW), FP16, kind="Internal").ap()
        m_shift = pM[:, 0:64].bitcast(BF16)
        m_yT = pM[:, 128:256]
        m_rank = pM[:, 256:264]
        m_gate = pM[:, 264:272]
        xs = nc.dram_tensor("xs", (NE * REGION + NT, ROW), FP32, kind="Internal").ap()
        zs = nc.dram_tensor("zs", (TOPK * TOKENS, D), FP32, kind="Internal").ap()
        m_out = pM[:, 384:512]

        consts_in = sem("consts_in")
        x_in = [sem("x_in_even"), sem("x_in_odd")]
        zeroed = sem("zeroed")
        weights_scaled = sem("weights_scaled")
        tables_cast = sem("tables_cast")
        setup_mm = sem("setup_mm")
        bias_done = sem("bias_done")
        kb_in = [sem("kb_in_even"), sem("kb_in_odd")]
        c_full = sem("c_full")
        vpad_out = sem("vpad_out")
        vwin_out = [sem("vwin_out_even"), sem("vwin_out_odd")]
        v_in = [sem("v_in_even"), sem("v_in_odd")]
        c_hi = sem("c_hi")
        c_lo = sem("c_lo")
        xc_done = sem("xc_done")
        scores_full = sem("scores_full")
        nmax_done = sem("nmax_done")
        shift_hi = sem("shift_hi")
        shift_done = sem("shift_done")
        shiftT_full = sem("shiftT_full")
        shiftT_done = sem("shiftT_done")
        shifted = sem("shifted")
        exp_done = sem("exp_done")
        probsT_full = sem("probsT_full")
        probsT_hi = sem("probsT_hi")
        probsT_lo = sem("probsT_lo")
        out_full = sem("out_full")
        rec_done = sem("rec_done")
        norm_done = sem("norm_done")
        attnT_done = sem("attnT_done")
        proj_full = sem("proj_full")
        r1_done = sem("r1_done")
        stats_done = sem("stats_done")
        mv_done = sem("mv_done")
        var_done = sem("var_done")
        rstd_done = sem("rstd_done")
        y_done = sem("y_done")
        ycopy_done = sem("ycopy_done")
        yT_full = sem("yT_full")
        yT_done = sem("yT_done")
        rank_read = sem("rank_read")
        lg_done = sem("lg_done")
        top_done = sem("top_done")
        topi_done = sem("topi_done")
        hot_done = sem("hot_done")
        hot16_done = sem("hot16_done")
        routed = sem("routed")
        picked_done = sem("picked_done")
        pos_done = sem("pos_done")
        marks_done = sem("marks_done")
        w_in = sem("w_in")
        w_up = sem("w_up")
        w_hi = sem("w_hi")
        w_lo = sem("w_lo")
        b2_in = sem("b2_in")
        b2_done = sem("b2_done")
        pads_out = sem("pads_out")
        tail_out = sem("tail_out")
        small = sem("small")
        count_full = sem("count_full")
        table = sem("table")
        table_done = sem("table_done")
        diff_done = sem("diff_done")
        exp2_done = sem("exp2_done")
        padpos_done = sem("padpos_done")
        wts_done = sem("wts_done")
        xg_in = [sem("xg_in_even"), sem("xg_in_odd")]
        xgT_full = sem("xgT_full")
        xh_done = sem("xh_done")
        xl_done = sem("xl_done")
        h_full = sem("h_full")
        gelu_done = sem("gelu_done")
        hh_done = sem("hh_done")
        hl_done = sem("hl_done")
        z_full = sem("z_full")
        z_done = sem("z_done")
        dstf_done = sem("dstf_done")
        dst_done = sem("dst_done")
        turn_done = sem("turn_done")
        zs_out = [sem("zs_out_even"), sem("zs_out_odd")]
        z_in = [sem("z_in_even"), sem("z_in_odd")]
        z1_done = sem("z1_done")
        z2_done = sem("z2_done")
        st2_done = sem("st2_done")
        mv2_done = sem("mv2_done")
        var2_done = sem("var2_done")
        rstd2_done = sem("rstd2_done")
        yout_done = sem("yout_done")
        yout_out = [sem("yout_out_even"), sem("yout_out_odd")]
        rows_out = [sem(f"rows_out_{n}") for n in range(BODY)]

        block = ctx.enter_context(nc.Block())

        def steps(eng, step, peel=0):
            for s in range(2 * BODY):
                step(s // BODY, s % BODY)
            with eng.Fori(2, TILES // BODY - peel) as i:
                for u in range(BODY):
                    step(i, u)
            for s in range(TILES - peel * BODY, TILES + LAG_R + 1):
                step(s // BODY, s % BODY)

        def in_steps(s):
            return not isinstance(s, int) or 0 <= s < SLOTS

        def in_chunks(c):
            return not isinstance(c, int) or 0 <= c < CHUNKS

        def by_twos(eng, step, total):
            for i in range(2):
                for u in range(2):
                    step(i, u)
            with eng.Fori(2, total // 2) as i:
                for u in range(2):
                    step(i, u)
            for u in range(2):
                step(total // 2, u)
            step(total // 2 + 1, 0)

        def expert_steps(eng, step):
            by_twos(eng, step, SLOTS)

        def chunk_steps(eng, step):
            by_twos(eng, step, CHUNKS)

        @block.sync
        def _(sp):
            sp.dma_start(stage[:, 0:128], c_ident).then_inc(consts_in, 16)
            sp.dma_start(stage[:, 128:384], c_seen).then_inc(consts_in, 16)
            sp.dma_start(stage[:, 384:448], c_mask).then_inc(consts_in, 16)
            sp.dma_start(stage[:, 448:464], c_heads).then_inc(consts_in, 16)
            for w, d in ((Wq, wq), (Wk, wk), (Wv, wv), (Wo, wo)):
                sp.dma_start(w[:, :], d).then_inc(consts_in, 16)
            for w, d in ((qb, bq), (kb, bk), (vb_col, bv)):
                sp.dma_start(w[:, :], d.rearrange("(a b) -> a b", b=1)).then_inc(consts_in, 16)
            sp.dma_start(stage[:, 464:592], c_tri).then_inc(consts_in, 16)
            sp.dma_start(tab[:, :], c_tab).then_inc(consts_in, 16)
            sp.dma_start(bo_row[:, :], bo.rearrange("(a b) -> a b", a=1)).then_inc(consts_in, 16)
            sp.dma_start(Wg[:, :], gate_w).then_inc(consts_in, 16)

            def load_x(s, p):
                sp.dma_start(xin[:, 2 * p:2 * p + 2, :], xt_dram[:, bass.ds(s, 2), :]).then_inc(x_in[p], 16)

            load_x(0, 0)
            sp.dma_start(b1t[:, :, :], b1).then_inc(w_in, 16)
            for n, w in enumerate((w1, w2)):
                for e in range(0, NE, 2):
                    sp.dma_start(w_raw[:, n * NE + e:n * NE + e + 2, :], w[:, e:e + 2, :]).then_inc(w_in, 16)

            sp.wait_ge(zeroed, 12 + 5)
            for row in (0, 32):
                sp.dma_start(b2raw[row:row + 1, :, :], b2.rearrange("(a e) d -> a e d", a=1)).then_inc(b2_in, 16)
            for p in range(2):
                sp.dma_start(vwin[p, 0:WINDOW, :], VB[0:WINDOW, 0, 0:2, :, :, :, :]).then_inc(vpad_out, 16)
            sp.wait_ge(vpad_out, 32)
            for n in range(NH):
                sp.dma_start(xs[NE * REGION + n * P:NE * REGION + (n + 1) * P, :], padrow[:, :]).then_inc(tail_out, 16)

            def step(i, u):
                s, b, p = BODY * i + u, 2 * i + u // 2, u // 2
                if u % 2 == 0:
                    x_next = fixed(sp, s + 2)
                    if live(s) and live(s + 2):
                        reach(sp, xc_done, s)
                        load_x(x_next, 1 - p)
                    if live(s - 2):
                        reach(sp, vwin_out[1 - p], 16 * (i + (u - 2) // BODY + 1))
                        for par in range(2):
                            src = view(vwin[1 - p, 0:2 * WINDOW, par * VROW // 2:(par + 1) * VROW // 2], [[WINDOW * VROW, TPB * NJ], [1, VROW // 2]])
                            sp.dma_start(VB[64 * par:64 * par + 64, 1 - p, :, :, :, :, :], src).then_inc(v_in[1 - p], 16)
                elif live(s):
                    reach(sp, c_lo, 2 * b + 1)
                    for h in range(H):
                        r = slice(h * HD, (h + 1) * HD)
                        sp.dma_start(KB[r, p, :, h, WINDOW:], k_nat[r, p, :, :]).then_inc(kb_in[p], 16)
                    reach(sp, c_lo, 2 * b + 2)
                    sp.dma_start(vwin[p, WINDOW:, :].rearrange("(n t) c -> t n c", n=TPB),
                                 v_nat[:, p, :, :, :, :, :, :].rearrange("t n a b c d e -> t n (a b c d e)")).then_inc(vwin_out[p], 16)
            steps(sp, step, peel=1)

            for n in range(BODY):
                sp.wait_ge(rows_out[n], 2 * 16 * CHUNKS)
            sp.wait_ge(pads_out, 16 * NH * NE)
            sp.wait_ge(tail_out, 16 * NH)
            sp.wait_ge(table_done, 1)

            def load_rows(i, u):
                s = 2 * i + u
                if in_steps(s):
                    row = sp.value_load(start_i[0:1, bass.ds(s, 1)], min_val=0, max_val=NE * REGION)
                    reach(sp, dstf_done, s - 1)
                    sp.dma_start(xg[:, u, :, :], xs[bass.ds(row, NT), :].rearrange("(n p) c -> p n c", p=P)).then_inc(xg_in[u], 16)
            expert_steps(sp, load_rows)

            for n in range(2):
                sp.wait_ge(zs_out[n], 16 * NH * SLOTS // 2)
            zs_t = zs.rearrange("(k t p) d -> p k t d", k=TOPK, p=P)

            def chunk(i, u):
                c = 2 * i + u
                if in_chunks(c):
                    at = fixed(sp, c * CH)
                    reach(sp, z2_done, CH * (c - 1))
                    for k in range(TOPK):
                        sp.dma_start(zin[:, u, k, :, :], zs_t[:, k, bass.ds(at, CH), :]).then_inc(z_in[u], 16)
                if in_chunks(c - 2):
                    at = fixed(sp, (c - 2) * CH)
                    reach(sp, yout_done, c - 1)
                    sp.dma_start(out_t[:, bass.ds(at, CH), :], yout[:, u, :, :]).then_inc(yout_out[u], 16)
            chunk_steps(sp, chunk)
            for n in range(2):
                sp.wait_ge(yout_out[n], 16 * CHUNKS // 2)

        @block.gpsimd
        def _(pool):
            pool.memset(KB[:, :, :, :, :], 0.0).then_inc(zeroed, 1)
            pool.memset(v_nat[:, :, :, :, :, :, :, :], 0.0).then_inc(zeroed, 1)
            pool.memset(VB[0:WINDOW, 0, :, :, :, :, :], 0.0).then_inc(zeroed, 1)
            pool.memset(shift[:, :, :], 0.0).then_inc(zeroed, 1)
            pool.memset(ones_row[:, :], 1.0).then_inc(zeroed, 1)
            pool.memset(y_new[:, :, :], 0.0).then_inc(zeroed, 1)
            pool.memset(padrow[:, :], 0.0).then_inc(zeroed, 1)
            pool.memset(neg_half[:, :], -0.5).then_inc(zeroed, 1)
            pool.memset(wup[:, :], WUP).then_inc(zeroed, 1)
            pool.memset(b2h[:, :, :], 0.0).then_inc(zeroed, 1)
            pool.memset(b2raw[:, :, :], 0.0).then_inc(zeroed, 1)
            pool.memset(eps[:, :], EPS).then_inc(zeroed, 1)
            pool.wait_ge(zeroed, 12)
            pool.memset(padrow[:, C_ID:C_ID + 1], NOWHERE).then_inc(zeroed, 1)
            for par in range(2):
                for p in range(2):
                    pool.memset(v_nat[:, p, :, par, 0, par, :, VW - 1], UP).then_inc(zeroed, 1)
            pool.wait_ge(bias_done, 1)

            def split_weights(k):
                n = bass.ds(k, 1)
                flat = lambda w: w[:, n, :].rearrange("p a f -> p (a f)")
                nc.gpsimd.tensor_tensor(flat(w_raw), flat(w_raw), view(wup[:, :], [[0, F]]), ALU.mult).then_inc(w_up, 1)
                reach(pool, w_up, k + 1)
                nc.gpsimd.tensor_copy(flat(w_hi16), flat(w_raw)).then_inc(w_hi, 1)
                reach(pool, w_hi, k + 1)
                nc.gpsimd.tensor_tensor(flat(w_lo16), flat(w_raw), flat(w_hi16), ALU.subtract).then_inc(w_lo, 1)

            def step(i, u):
                s, tO, tR = BODY * i + u, BODY * i + u - LAG_O, BODY * i + u - LAG_R
                if live(s):
                    reach(pool, x_in[u // 2], 16 * (i + 1))
                    reach(pool, c_full, 3 * (2 * i + u // 2) + 1)
                if live(tR):
                    reach(pool, ycopy_done, tR + 1)
                    reach(pool, pos_done, tR + 1)
                if live(s):
                    nc.gpsimd.tensor_tensor(Y[:, bass.ds(s, 1), :].rearrange("p a d -> p (a d)"), xin[:, u, :], out_bias[:, :],
                                            ALU.add).then_inc(xc_done, 1)
                if live(tR):
                    slot = (u - LAG_R) % BODY
                    for k in range(TOPK):
                        nc.gpsimd.indirect_dma_start(xs, bass.IndirectOffsetOnAxis(ap=pos[:, slot, k:k + 1], axis=0),
                                                     y_new[:, slot, :], None).then_inc(rows_out[slot], 16)
                if live(tO):
                    q = u % 2
                    reach(pool, mv_done, tO + 1)
                    nc.gpsimd.tensor_tensor(var_eps[:, q, :], mv[:, q, 1:2], eps[:, :], ALU.add).then_inc(var_done, 1)
                    reach(pool, var_done, tO + 1)
                    nc.gpsimd.tensor_tensor(rstd[:, q, :], var_eps[:, q, :], neg_half[:, :], ALU.pow).then_inc(rstd_done, 1)
                    reach(pool, y_done, tO + 1)
                    nc.gpsimd.tensor_copy(Y[:, bass.ds(tO, 1), :].rearrange("p a d -> p (a d)"), y_new[:, u, 0:D])
                    nc.gpsimd.tensor_copy(y_new[:, u, C_ID:C_ID + 1], tab[:, bass.ds(T_TOK + tO, 1)]).then_inc(ycopy_done, 1)
            for s in range(2 * BODY):
                step(s // BODY, s % BODY)
            pool.wait_ge(w_in, 16 * (1 + NE))
            with pool.Fori(2, 2 + NE) as i:
                for u in range(BODY):
                    step(i, u)
                    if u % 2:
                        split_weights((i - 2) * 2 + u // 2)
            with pool.Fori(2 + NE, TILES // BODY) as i:
                for u in range(BODY):
                    step(i, u)
            for s in range(TILES, TILES + LAG_R + 1):
                step(s // BODY, s % BODY)

            pool.wait_ge(padpos_done, 1)
            for n in range(NH):
                for e in range(NE):
                    nc.gpsimd.indirect_dma_start(xs, bass.IndirectOffsetOnAxis(ap=padpos[:, n, e:e + 1], axis=0), padrow[:, :], None)\
                      .then_inc(pads_out, 16)

            def scatter(i, u):
                j = 2 * i + u
                if in_steps(j):
                    reach(pool, dst_done, j + 1)
                    reach(pool, z_done, j + 1)
                    reach(pool, turn_done, j)
                    nc.gpsimd.tensor_tensor(turn[:, :], neg_half[:, :], neg_half[:, :], ALU.mult).then_inc(turn_done, 1)
                    for n in range(NH):
                        nc.gpsimd.indirect_dma_start(zs, bass.IndirectOffsetOnAxis(ap=dst[:, u, n:n + 1], axis=0), zrow[:, u, n, :], None,
                                                     bounds_check=TOPK * TOKENS - 1, oob_is_err=False).then_inc(zs_out[u], 16)
            for u in range(2):
                scatter(0, u)
            with pool.Fori(1, SLOTS // 2) as i:
                for u in range(2):
                    scatter(i, u)

            def root(i, u):
                c = 2 * i + u - 1
                w = 1 - u
                if in_chunks(c):
                    reach(pool, mv2_done, c + 1)
                    nc.gpsimd.tensor_tensor(var2[:, w, :], mv2[:, w, :, 1], view(eps[:, :], [[0, CH]]), ALU.add).then_inc(var2_done, 1)
                    reach(pool, var2_done, c + 1)
                    nc.gpsimd.tensor_tensor(rstd2[:, w, :], var2[:, w, :], view(neg_half[:, :], [[0, CH]]), ALU.pow).then_inc(rstd2_done, 1)
            chunk_steps(pool, root)

        @block.scalar
        def _(act):
            act.wait_ge(consts_in, 16 * 15)
            for w in (Wq[:, :], Wk[:, :], Wv[:, :], qb[:, :], kb[:, :]):
                nc.scalar.mul(w, w, UP).then_inc(weights_scaled, 1)
            act.wait_ge(setup_mm, 1)
            nc.scalar.copy(out_bias[:, :], pM[:, 0:128]).then_inc(bias_done, 1)

            def step(i, u):
                s, b, p = BODY * i + u, 2 * i + u // 2, u // 2
                tS, tP, tY, tO = s - LAG_S, s - LAG_P, s - LAG_Y, s - LAG_O
                if live(tY):
                    reach(act, yT_full, tY + 1)
                    nc.scalar.copy(yT[:, (u - LAG_Y) % 2, :], m_yT).then_inc(yT_done, 1)
                if live(s):
                    if u % 2 == 0:
                        reach(act, c_full, 3 * b + 1)
                        nc.scalar.copy(xT[:, p, :], pC[:, 0:S]).then_inc(c_hi, 1)
                    else:
                        reach(act, c_full, 3 * b + 3)
                        reach(act, vwin_out[p], 16 * i)
                        for n in range(TPB):
                            last = nc.scalar.copy(view(v_nat[:, p, n, 0, 0, 0, 0, :], V_DIAG), view(pC[:, n * D:(n + 1) * D], V_FLAT))
                        last.then_inc(c_hi, 1)
                if live(tS):
                    reach(act, shiftT_full, tS + 1)
                    nc.scalar.copy(shiftT[:, u % 2, :], m_shift).then_inc(shiftT_done, 1)
                if live(tP):
                    reach(act, probsT_full, tP + 1)
                    nc.scalar.copy(PTh[:, (u - LAG_P) % 2, :, :, :].rearrange("p a b c -> p (a b c)"), pT[:, :, :].rearrange("p a b -> p (a b)")).then_inc(probsT_hi, 1)
                if live(tS):
                    reach(act, shifted, tS + 1)
                    nc.scalar.activation(E[:, u % 2, :], pS[:, :, :], ACT.Exp, scale=SCORE_SCALE).then_inc(exp_done, 1)
                if live(s):
                    if u % 2 == 0:
                        reach(act, c_full, 3 * b + 2)
                        nc.scalar.activation(q_hi[:, p, :], pC[:, 0:S], ACT.Identity, bias=qb[:, :])
                        nc.scalar.activation(k_nat[:, p, 0, :], pC[:, S:2 * S], ACT.Identity, bias=kb[:, :]).then_inc(c_hi, 1)
            steps(act, step)

            act.wait_ge(diff_done, 1)
            nc.scalar.activation(wtmp[:, 1, :], wtmp[:, 0, :], ACT.Exp).then_inc(exp2_done, 1)
            act.wait_ge(table_done, 1)

            def expert(i, u):
                s = 2 * i + u
                if in_steps(s):
                    reach(act, xgT_full, s + 1)
                    nc.scalar.mul(xh[:, u, :], pC[:, 0:NT], UP).then_inc(xh_done, 1)
                g, w = s - 1, 1 - u
                if in_steps(g):
                    e = act.value_load(expert_i[0:1, bass.ds(g, 1)], min_val=0, max_val=NE - 1)
                    bank = (pS, pT)[w]
                    for half in range(2):
                        reach(act, h_full, 2 * g + half + 1)
                        reach(act, hl_done, 2 * (g - 2) + half + 1)
                        for k in range(2):
                            c = 2 * half + k
                            last = nc.scalar.activation(G[:, w, c, :], bank[:, half, k * NT:(k + 1) * NT], ACT.Gelu, scale=1 / (UP * WUP),
                                                        bias=b1t[:, bass.ds(e, 1), c])
                        last.then_inc(gelu_done, 1)
                z = s - 2
                if in_steps(z):
                    reach(act, z_full, z + 1)
                    reach(act, zs_out[u], 16 * NH * (i - 1))
                    nc.scalar.mul(zrow[:, u, :, :].rearrange("p n d -> p (n d)"), pO[:, u, 0:NH * D], 1 / (UP * WUP)).then_inc(z_done, 1)
            expert_steps(act, expert)

        @block.vector
        def _(dve):
            dve.wait_ge(consts_in, 16 * 15)
            nc.vector.tensor_copy(ident[:, :], stage[:, 0:128]).then_inc(tables_cast, 1)
            nc.vector.tensor_copy(ident16[:, :], stage[:, 0:128]).then_inc(tables_cast, 1)
            nc.vector.tensor_copy(seen[:, :, :], stage[:, 128:384]).then_inc(tables_cast, 1)
            nc.vector.tensor_copy(mask[:, :, :], view(stage[:, 384:448], [[0, HALF], [1, KEYS]])).then_inc(tables_cast, 1)
            nc.vector.tensor_copy(tri[:, :], stage[:, 464:592]).then_inc(tables_cast, 1)
            nc.vector.memset(ones_f[:, :], 1.0)
            nc.vector.memset(ones16[:, :], 1.0).then_inc(tables_cast, 1)
            nc.vector.memset(seen16[:, :, :], 0.0).then_inc(tables_cast, 1)
            nc.vector.tensor_copy(heads[:, :, :], view(stage[:, 448:464], [[1, H], [0, KEYS]])).then_inc(tables_cast, 1)

            dve.wait_ge(zeroed, 12 + 5)
            dve.wait_ge(b2_in, 32)
            nc.vector.memset(ones2[:, :], UP * WUP / BUP)
            nc.vector.tensor_scalar(b2h[0:64, :, :], b2raw[:, :, :], BUP, None, ALU.mult).then_inc(b2_done, 1)
            dve.wait_ge(b2_done, 1)
            nc.vector.scalar_tensor_tensor(out=b2h[32:64, :, :], in0=b2raw[32:64, :, :], scalar=BUP, in1=b2h[32:64, :, :],
                                           op0=ALU.mult, op1=ALU.subtract).then_inc(b2_done, 1)

            def step(i, u):
                s, b, p = BODY * i + u, 2 * i + u // 2, u // 2
                tS, tP, tO, tY, tR = s - LAG_S, s - LAG_P, s - LAG_O, s - LAG_Y, s - LAG_R
                q = u % 2
                if live(tO):
                    reach(dve, out_full, tO + 1)
                    o = pO[:, :, 0:NJ * 2 * VW].rearrange("p a (j c) -> p a j c", c=VW)
                    nc.vector.reciprocal(rec[:, q, :, :], o[:, :, :, VW - 1]).then_inc(rec_done, 1)
                    reach(dve, rec_done, tO + 1)
                    for hp in range(4):
                        r = slice(32 * hp, 32 * hp + 32)
                        last = nc.vector.tensor_tensor(
                            O2[r, q, :, :, :].rearrange("p a j (b d) -> p a (j b) d", d=HD), o[r, :, :, hp * HD:hp * HD + HD],
                            view(rec[r, q, :, :], [[NJ * 2, 2], [1, NJ * 2], [0, HD]]), ALU.mult)
                    last.then_inc(norm_done, 1)
                    reach(dve, norm_done, tO + 1)
                    nc.vector.transpose(attnT[:, q, :], O2[:, q, :, :, :].rearrange("p a j c -> p j a c")).then_inc(attnT_done, 1)
                if live(tS):
                    reach(dve, scores_full, tS + 1)
                    nc.vector.tensor_reduce(out=nmax[:, q, :], in_=pS[:, :, :].rearrange("p a (h k) -> p (a h) k", k=KEYS),
                                            axis=AX.X, op=ALU.max, negate=True).then_inc(nmax_done, 1)
                    reach(dve, nmax_done, tS + 1)
                    nc.vector.tensor_scalar(shift[:, q, 0:H], nmax[:, q, :], LIFT / SCORE_SCALE, None, ALU.add).then_inc(shift_hi, 1)
                    reach(dve, shift_hi, tS + 1)
                    nc.vector.scalar_tensor_tensor(out=shift[:, q, 32:32 + H], in0=nmax[:, q, :], scalar=LIFT / SCORE_SCALE,
                                                   in1=shift[:, q, 0:H], op0=ALU.add, op1=ALU.subtract).then_inc(shift_done, 1)
                if live(tR):
                    w = (u - LAG_R) % 2
                    reach(dve, yT_full, tR + 2)
                    if live(tR + 1):
                        reach(dve, yT_done, tR + 2)
                    nc.vector.tensor_tensor(where[:, w, :], m_rank, tab[:, T_BASE:T_BASE + NE], ALU.add).then_inc(rank_read, 1)
                    reach(dve, rank_read, tR + 1)
                    nc.vector.tensor_tensor(picked[:, w, :, :], hot[:, w, :, :], view(where[:, w, :], [[0, TOPK], [1, NE]]), ALU.mult).then_inc(picked_done, 1)
                    reach(dve, picked_done, tR + 1)
                    with nc.allow_low_precision(reason="whole numbers below 2 ** 24"):
                        nc.vector.tensor_reduce(out=pos[:, (u - LAG_R) % BODY, :], in_=picked[:, w, :, :], axis=AX.X, op=ALU.add).then_inc(pos_done, 1)
                if live(tP):
                    w = (u - LAG_P) % 2
                    reach(dve, probsT_hi, tP + 1)
                    nc.vector.tensor_tensor(PTl[:, w, :, :, :].rearrange("p a b c -> p (a b c)"), pT[:, :, :].rearrange("p a b -> p (a b)"),
                                            PTh[:, w, :, :, :].rearrange("p a b c -> p (a b c)"), ALU.subtract).then_inc(probsT_lo, 1)
                w = (u - LAG_Y) % 2
                if live(tY):
                    reach(dve, proj_full, tY + 2)
                    nc.vector.tensor_copy(lg[:, w, :], m_gate).then_inc(lg_done, 1)
                if live(tO):
                    reach(dve, proj_full, tO + 1)
                    reach(dve, xc_done, tO + 1)
                if live(tY):
                    reach(dve, lg_done, tY + 1)
                if live(tO):
                    nc.vector.tensor_tensor(r1[:, q, :], m_out, Y[:, bass.ds(tO, 1), :].rearrange("p a d -> p (a d)"), ALU.add).then_inc(r1_done, 1)
                if live(tY):
                    nc.vector.max(top[:, w, :], lg[:, w, :]).then_inc(top_done, 1)
                if live(tO):
                    reach(dve, r1_done, tO + 1)
                if live(tY):
                    reach(dve, top_done, tY + 1)
                if live(tO):
                    nc.vector.bn_stats(stats[:, q, :], r1[:, q, :]).then_inc(stats_done, 1)
                if live(tY):
                    nc.vector.max_index(topi[:, w, :], top[:, w, :], lg[:, w, :]).then_inc(topi_done, 1)
                    nc.vector.tensor_copy(vals[:, bass.ds(tY, 1), :].rearrange("p a d -> p (a d)"), top[:, w, 0:TOPK])
                if live(s):
                    reach(dve, c_hi, 3 * b + 2 + u % 2)
                if live(tO):
                    reach(dve, stats_done, tO + 1)
                if live(s) and u % 2 == 0:
                    nc.vector.scalar_tensor_tensor(out=q_lo[:, p, :], in0=pC[:, 0:S], scalar=qb[:, :], in1=q_hi[:, p, :],
                                                   op0=ALU.add, op1=ALU.subtract)
                    nc.vector.scalar_tensor_tensor(out=k_nat[:, p, 1, :], in0=pC[:, S:2 * S], scalar=kb[:, :], in1=k_nat[:, p, 0, :],
                                                   op0=ALU.add, op1=ALU.subtract).then_inc(c_lo, 1)
                elif live(s):
                    for n in range(TPB):
                        last = nc.vector.tensor_tensor(view(v_nat[:, p, n, 0, 1, 0, 0, :], V_DIAG), view(pC[:, n * D:(n + 1) * D], V_FLAT),
                                                       view(v_nat[:, p, n, 0, 0, 0, 0, :], V_DIAG), ALU.subtract)
                    last.then_inc(c_lo, 1)
                if live(tO):
                    nc.vector.bn_aggr(mv[:, q, :], stats[:, q, :]).then_inc(mv_done, 1)
                if live(tY):
                    reach(dve, topi_done, tY + 1)
                    nc.vector.tensor_tensor(hot[:, w, :, :], view(tab[:, T_E:T_E + NE], [[0, TOPK], [1, NE]]),
                                            view(topi[:, w, :], [[1, TOPK], [0, NE]]), ALU.is_equal).then_inc(hot_done, 1)
                    nc.vector.tensor_copy(y_new[:, (u - LAG_Y) % BODY, C_E1:C_E1 + 1], topi[:, w, 0:1]).then_inc(marks_done, 1)
                    reach(dve, hot_done, tY + 1)
                    nc.vector.tensor_tensor(hot16[:, w, :], hot[:, w, 0, :], hot[:, w, 1, :], ALU.add).then_inc(hot16_done, 1)
                    reach(dve, hot16_done, tY + 1)
                    nc.vector.tensor_tensor(seen16[:, w, :], seen16[:, 1 - w, :], hot16[:, w, :], ALU.add).then_inc(routed, 1)
                if live(tO):
                    reach(dve, rows_out[u], 2 * 16 * (i - 1))
                    reach(dve, rstd_done, tO + 1)
                    nc.vector.tensor_scalar(y_new[:, u, 0:D], r1[:, q, :], mv[:, q, 0:1], rstd[:, q, :], ALU.subtract, ALU.mult).then_inc(y_done, 1)
            steps(dve, step)

            made = [0]

            def then(ins):
                made[0] += 1
                ins.then_inc(table, 1)
                dve.wait_ge(table, made[0])

            dve.wait_ge(count_full, 1)
            then(nc.vector.tensor_copy(count[:, :], pM[:, 0:NE]))
            nc.vector.tensor_tensor(padpos[:, :, :], tab[:, T_PAD:T_PAD + NH * NE].rearrange("p (n e) -> p n e", n=NH),
                                    view(count[:, :], [[0, NH], [1, NE]]), ALU.add).then_inc(padpos_done, 1)
            then(nc.vector.tensor_scalar(nt_i[:, :], count[:, :], float(NT - 1), None, ALU.add))
            then(nc.vector.tensor_scalar(nt_s[:, :], nt_i[:, :], NT.bit_length() - 1, None, ALU.logical_shift_right))
            then(nc.vector.tensor_copy(nt[:, :], nt_s[:, :]))
            then(nc.vector.tensor_tensor_scan(ntc[:, :], view(ones_f[:, :], [[0, NE]]), nt[:, :], 0.0, ALU.mult, ALU.add))
            then(nc.vector.tensor_tensor(past[:, :, :], view(tab[:, T_SLOT:T_SLOT + SLOTS], [[0, NE], [1, SLOTS]]),
                                         view(ntc[:, :], [[1, NE], [0, SLOTS]]), ALU.is_ge))
            then(nc.vector.tensor_reduce(out=expert[:, :], in_=past[:, :, :].rearrange("p e s -> p s e"), axis=AX.X, op=ALU.add))
            then(nc.vector.tensor_scalar(expert_i[:, :], expert[:, :], float(NE - 1), None, ALU.min))
            then(nc.vector.tensor_scalar(step_rows[:, :], nt[:, :], -float(NT), float(REGION), ALU.mult, ALU.add))
            then(nc.vector.tensor_tensor(past[:, :, :], past[:, :, :], view(step_rows[:, :], [[1, NE], [0, SLOTS]]), ALU.mult))
            then(nc.vector.tensor_reduce(out=start_f[:, 0, :], in_=past[:, :, :].rearrange("p e s -> p s e"), axis=AX.X, op=ALU.add))
            then(nc.vector.tensor_tensor(start_f[:, 1, :], start_f[:, 0, :], tab[:, T_SLOT + SLOTS:T_SLOT + 2 * SLOTS], ALU.add))
            nc.vector.tensor_scalar(start_i[:, :], start_f[:, 1, :], float(NE * REGION), None, ALU.min).then_inc(table_done, 1)
            nc.vector.tensor_tensor(wtmp[:, 0, :], vals[:, :, 1], vals[:, :, 0], ALU.subtract).then_inc(diff_done, 1)
            dve.wait_ge(exp2_done, 1)
            then(nc.vector.tensor_scalar(wtmp[:, 2, :], wtmp[:, 1, :], 1.0, None, ALU.add))
            then(nc.vector.reciprocal(wts[:, :, 0], wtmp[:, 2, :]))
            then(nc.vector.tensor_tensor(wts[:, :, 1], wtmp[:, 1, :], wts[:, :, 0], ALU.mult))

            def expert_low(i, u):
                s = 2 * i + u
                if in_steps(s):
                    reach(dve, xh_done, s + 1)
                    nc.vector.scalar_tensor_tensor(out=xl[:, u, :], in0=pC[:, 0:NT], scalar=UP, in1=xh[:, u, :],
                                                   op0=ALU.mult, op1=ALU.subtract).then_inc(xl_done, 1)
                    reach(dve, xg_in[u], 16 * (i + 1))
                    reach(dve, dst_done, s - 1)
                    nc.vector.scalar_tensor_tensor(out=dst_f[:, u, :], in0=xg[:, u, :, C_E1], scalar=expert[:, bass.ds(s, 1)],
                                                   in1=xg[:, u, :, C_ID], op0=ALU.not_equal, op1=ALU.add).then_inc(dstf_done, 1)
                g, w = s - 1, 1 - u
                if in_steps(g):
                    for half in range(2):
                        hs = slice(2 * half, 2 * half + 2)
                        reach(dve, gelu_done, 2 * g + half + 1)
                        reach(dve, z_full, g - 1)
                        nc.vector.tensor_scalar(Hh[:, w, hs, :], G[:, w, hs, :], UP, None, ALU.mult).then_inc(hh_done, 1)
                        reach(dve, hh_done, 2 * g + half + 1)
                        nc.vector.scalar_tensor_tensor(out=Hl[:, w, hs, :], in0=G[:, w, hs, :], scalar=UP, in1=Hh[:, w, hs, :],
                                                       op0=ALU.mult, op1=ALU.subtract).then_inc(hl_done, 1)
                    reach(dve, zs_out[w], 16 * NH * (i if u else i - 1))
                    reach(dve, dstf_done, g + 1)
                    nc.vector.tensor_scalar(dst[:, w, :], dst_f[:, w, :], float(TOKENS), None, ALU.mult).then_inc(dst_done, 1)
            expert_steps(dve, expert_low)

            def combine(i, u):
                c = 2 * i + u
                if in_chunks(c):
                    reach(dve, z_in[u], 32 * (i + 1))
                    reach(dve, yout_done, c - 1)
                    for n in range(CH):
                        t = c * CH + n
                        nc.vector.scalar_tensor_tensor(out=zsum[:, u, n, :], in0=zin[:, u, 0, n, :], scalar=wts[:, bass.ds(t, 1), 0],
                                                       in1=Y[:, bass.ds(t, 1), :].rearrange("p a d -> p (a d)"),
                                                       op0=ALU.mult, op1=ALU.add).then_inc(z1_done, 1)
                    for n in range(CH):
                        t = c * CH + n
                        reach(dve, z1_done, t + 1)
                        nc.vector.scalar_tensor_tensor(out=zsum[:, u, n, :], in0=zin[:, u, 1, n, :], scalar=wts[:, bass.ds(t, 1), 1],
                                                       in1=zsum[:, u, n, :], op0=ALU.mult, op1=ALU.add).then_inc(z2_done, 1)
                    for n in range(CH):
                        reach(dve, z2_done, c * CH + n + 1)
                        nc.vector.bn_stats(st2[:, u, n, :], zsum[:, u, n, :]).then_inc(st2_done, 1)
                g, w = c - 1, 1 - u
                if in_chunks(c):
                    reach(dve, st2_done, CH * (c + 1))
                if in_chunks(g):
                    reach(dve, rstd2_done, g + 1)
                    reach(dve, yout_out[w], 16 * (i if u else i - 1))
                    for n in range(CH):
                        last = nc.vector.tensor_scalar(yout[:, w, n, :], zsum[:, w, n, :], mv2[:, w, n, 0:1], rstd2[:, w, n:n + 1], ALU.subtract, ALU.mult)
                    last.then_inc(yout_done, 1)
                if in_chunks(c):
                    for n in range(CH):
                        last = nc.vector.bn_aggr(mv2[:, u, n, :], st2[:, u, n, :])
                    last.then_inc(mv2_done, 1)
            chunk_steps(dve, combine)

        @block.tensor
        def _(pe):
            pe.wait_ge(zeroed, 12 + 5)
            pe.wait_ge(weights_scaled, 5)
            pe.wait_ge(tables_cast, 8)
            nc.tensor.matmul(pM[:, 0:128], view(vb_col[:, :], [[0, P]]), Wo[:, :], start=True, stop=False)
            nc.tensor.matmul(pM[:, 0:128], ones_row[:, :], bo_row[:, :], start=False, stop=True).then_inc(setup_mm, 1)
            pe.wait_ge(bias_done, 1)

            def scores(i, u, t):
                p = ((u - LAG_S) // 2) % 2
                first = u % 2
                reach(pe, kb_in[p], 256 * (i + (u - LAG_S) // BODY + 1))
                reach(pe, exp_done, t)
                for a in range(2):
                    nc.tensor.matmul(pS[:, a, :], seen[:, first, :], mask[:, :, :], start=True, stop=False, skip_group_check=True)
                for qs, part in ((q_hi, 0), (q_hi, 1), (q_lo, 0)):
                    for a in range(2):
                        for j in range(NJ):
                            c = first * P + j * WINDOW
                            last = nc.tensor.matmul(pS[32 * j:32 * j + 32, a, :], qs[:, p, c:c + WINDOW],
                                                    KB[:, p, part, a * HALF:(a + 1) * HALF, c:c + KEYS],
                                                    start=False, stop=qs is q_lo, skip_group_check=True)
                last.then_inc(scores_full, 1)

            def step(i, u):
                s, b, p = BODY * i + u, 2 * i + u // 2, u // 2
                tS, tP, tO, tY, tR = s - LAG_S, s - LAG_P, s - LAG_O, s - LAG_Y, s - LAG_R
                if live(tS):
                    scores(i, u, tS)
                if live(tY):
                    reach(pe, y_done, tY + 1)
                    reach(pe, r1_done, tY + 1)
                if live(tR):
                    reach(pe, lg_done, tR + 1)
                if live(tY):
                    last = nc.tensor.transpose(m_yT, y_new[:, (u - LAG_Y) % BODY, 0:D], ident[:, :])
                if live(tR):
                    w = (u - LAG_R) % 2
                    reach(pe, routed, tR + 1)
                    nc.tensor.matmul(m_rank, tri[:, :], hot16[:, w, :], start=True, stop=False)
                    last = nc.tensor.matmul(m_rank, ones16[:, :], seen16[:, 1 - w, :], start=False, stop=True)
                if live(tY) or live(tR):
                    last.then_inc(yT_full, 1)
                if live(s):
                    if u % 2 == 0:
                        reach(pe, c_hi, 3 * b)
                        reach(pe, c_lo, 2 * b)
                        reach(pe, x_in[p], 16 * (i + 1))
                        for n in range(TPB):
                            last = nc.tensor.transpose(pC[:, n * P:(n + 1) * P], xin[:, u + n, :], ident[:, :])
                        last.then_inc(c_full, 1)
                    else:
                        reach(pe, c_hi, 3 * b + 2)
                        reach(pe, c_lo, 2 * b + 1)
                        for n in range(TPB):
                            last = nc.tensor.matmul(pC[:, n * P:(n + 1) * P], xT[:, p, n * P:(n + 1) * P], Wv[:, :], start=True, stop=True)
                        last.then_inc(c_full, 1)
                if live(tP):
                    reach(pe, exp_done, tP + 1)
                    reach(pe, probsT_lo, tP)
                    for k in range(8):
                        last = nc.tensor.transpose(view(pT[:, k % 2, :], [[P, NJ], [1, WINDOW]], (k // 2) * WINDOW),
                                                   E[:, (u - LAG_P) % 2, k * P:(k + 1) * P], ident[:, :])
                    last.then_inc(probsT_full, 1)
                if live(tY):
                    reach(pe, yT_done, tY + 1)
                if live(tR):
                    reach(pe, rank_read, tR + 1)
                if live(tS):
                    reach(pe, shift_done, tS + 1)
                    nc.tensor.transpose(m_shift, shift[:, u % 2, :], ident16[:, :]).then_inc(shiftT_full, 1)
                    reach(pe, shiftT_done, tS + 1)
                    for a in range(2):
                        last = nc.tensor.matmul(pS[:, a, :], shiftT[:, u % 2, :], heads[:, a * HALF:(a + 1) * HALF, :],
                                                start=False, stop=True, skip_group_check=True)
                    last.then_inc(shifted, 1)
                if live(tO):
                    reach(pe, attnT_done, tO + 1)
                    last = nc.tensor.matmul(m_out, attnT[:, u % 2, :], Wo[:, :], start=True, stop=True)
                if live(tY):
                    last = nc.tensor.matmul(m_gate, yT[:, (u - LAG_Y) % 2, :], Wg[:, :], start=True, stop=True)
                if live(tO) or live(tY):
                    last.then_inc(proj_full, 1)
                if live(s):
                    if u % 2 == 0:
                        reach(pe, c_hi, 3 * b + 1)
                        nc.tensor.matmul(pC[:, 0:S], Wq[:, :], xT[:, p, :], start=True, stop=True)
                        nc.tensor.matmul(pC[:, S:2 * S], Wk[:, :], xT[:, p, :], start=True, stop=True).then_inc(c_full, 1)
                if live(tP):
                    w = (u - LAG_P) % 2
                    reach(pe, probsT_lo, tP + 1)
                    reach(pe, norm_done, tP)
                    pP = ((u - LAG_P) // 2) % 2
                    reach(pe, v_in[pP], 32 * (i + (u - LAG_P) // BODY + 1))
                    for a in range(2):
                        for vi, (pt, vb) in enumerate(((PTh, 0), (PTh, 1), (PTl, 0))):
                            for j in range(NJ):
                                last = nc.tensor.matmul(pO[:, a, j * 2 * VW:(j + 1) * 2 * VW],
                                                        pt[:, w, a, j, :],
                                                        VB[:, pP, ((u - LAG_P) % 2) * NJ + j, vb, :, a, :], start=(vi == 0 and j == 0), stop=(vi == 2),
                                                        skip_group_check=True)
                    last.then_inc(out_full, 1)
            steps(pe, step)

            pe.wait_ge(routed, TILES)
            pe.wait_ge(rank_read, TILES)
            pe.wait_ge(lg_done, TILES)
            nc.tensor.matmul(pM[:, 0:NE], ones16[:, :], seen16[:, (TILES - 1) % 2, :], start=True, stop=True).then_inc(count_full, 1)
            pe.wait_ge(table_done, 1)
            pe.wait_ge(w_lo, 2 * NE)
            pe.wait_ge(b2_done, 2)

            def expert(i, u):
                s = 2 * i + u
                if in_steps(s):
                    reach(pe, xg_in[u], 16 * (i + 1))
                    reach(pe, xl_done, s)
                    for n in range(NH):
                        last = nc.tensor.transpose(pC[:, n * P:(n + 1) * P], xg[:, u, n, 0:D], ident[:, :])
                    last.then_inc(xgT_full, 1)
                g, w = s - 1, 1 - u
                if in_steps(g):
                    e = pe.value_load(expert_i[0:1, bass.ds(g, 1)], min_val=0, max_val=NE - 1)
                    bank = (pS, pT)[w]
                    reach(pe, xl_done, g + 1)
                    reach(pe, gelu_done, 2 * (g - 1))
                    for c in range(FC):
                        o = bank[:, c // 2, (c % 2) * NT:(c % 2 + 1) * NT]
                        for m, (wt, xp) in enumerate(((w1h, xh), (w1h, xl), (w1l, xh))):
                            last = nc.tensor.matmul(o, wt[:, bass.ds(e, 1), c * P:(c + 1) * P].rearrange("p a f -> p (a f)"), xp[:, w, :],
                                                    start=m == 0, stop=m == 2)
                        if c % 2:
                            last.then_inc(h_full, 1)
                z = s - 2
                if in_steps(z):
                    e = pe.value_load(expert_i[0:1, bass.ds(z, 1)], min_val=0, max_val=NE - 1)
                    reach(pe, hl_done, 2 * z + 2)
                    reach(pe, z_done, z - 1)
                    for n in range(NH):
                        o = pO[:, u, n * D:(n + 1) * D]
                        nc.tensor.matmul(o, ones2[:, :], b2h[:, bass.ds(e, 1), :].rearrange("p a d -> p (a d)"), start=True, stop=False)
                        for c in range(FC):
                            for hp, wt in ((Hh, w2h), (Hh, w2l), (Hl, w2h)):
                                last = nc.tensor.matmul(o, hp[:, u, c, n * P:(n + 1) * P],
                                                        wt[:, bass.ds(e, 1), c, :].rearrange("p a d -> p (a d)"),
                                                        start=False, stop=(c == FC - 1 and wt is w2h and hp is Hl))
                    last.then_inc(z_full, 1)
            expert_steps(pe, expert)


def constants():
    seen = np.zeros((P, 2, P), np.float32)
    for c in range(P):
        seen[c % WINDOW, :, c] = 1
    seen[WINDOW, 0, 0:WINDOW] = 1
    mask = np.zeros((P, KEYS), np.float32)
    q, k = np.arange(WINDOW)[:, None], np.arange(KEYS)[None, :]
    ago = q + WINDOW - k
    mask[:WINDOW] = np.where((ago >= 0) & (ago < WINDOW), 0, NEG)
    mask[WINDOW, :WINDOW] = NEG
    heads = np.zeros((P, H), np.float32)
    for h in range(H):
        heads[h, h] = heads[32 + h, h] = 1
    t, e, r = np.arange(TILES), np.arange(NE), np.arange(P)[:, None]
    wide = lambda v: np.broadcast_to(np.asarray(v, np.float32), (P, len(v)))
    steps = np.arange(SLOTS)
    tab = np.concatenate([(t[None] * P + r) / TOKENS, wide(e * REGION), wide(e), e[None] * REGION + r, e[None] * REGION + P + r,
                          wide(steps), wide(steps * NT)], 1).astype(np.float32)
    return {"tri": np.triu(np.ones((P, P), np.float32), 1), "tab": tab, "ident": np.eye(P, dtype=np.float32), "seen": seen.reshape(P, -1), "mask": mask, "heads": heads}


def kernel(**inputs):
    import concourse.bacc as bacc
    from concourse.bass_utils import run_bass_kernel_spmd

    nc = bacc.Bacc("TRN2", target_bir_lowering=False, num_devices=1)
    a = {k: np.ascontiguousarray(v) for k, v in inputs.items()}
    arrays = {"x": a["L0_attn_x"], "wq": a["L0_attn_Wq"], "wk": a["L0_attn_Wk"],
              "wv": np.ascontiguousarray(a["L0_attn_Wv"].reshape(D, 4, 2, 2, HD).transpose(0, 3, 2, 1, 4).reshape(D, D)),
              "wo": a["L0_attn_Wo"], "bq": a["L0_attn_bq"], "bk": a["L0_attn_bk"], "bv": a["L0_attn_bv"], "bo": a["L0_attn_bo"],
              "gate_w": a["L0_ffn_gate_w"],
              "w1": np.ascontiguousarray(a["L0_ffn_w1"].transpose(1, 0, 2)),
              "b1": np.ascontiguousarray(a["L0_ffn_b1"].reshape(NE, FC, P).transpose(2, 0, 1)),
              "w2": np.ascontiguousarray(a["L0_ffn_w2"].reshape(NE, FC, P, D).transpose(2, 0, 1, 3).reshape(P, NE, FC * D)),
              "b2": a["L0_ffn_b2"]}
    tables = constants()
    arrays.update({"c_" + k: tables[k] for k in ("ident", "seen", "mask", "heads", "tri", "tab")})
    args = [nc.dram_tensor(k, v.shape, mybir.dt.from_np(v.dtype), kind="ExternalInput").ap() for k, v in arrays.items()]
    args.append(nc.dram_tensor("out", (B, S, D), FP32, kind="ExternalOutput").ap())
    build(nc, *args)
    r = run_bass_kernel_spmd(nc, [arrays], core_ids=[0])
    return r.results[0]["out"]
```
